# Optimizing a Trainium2 kernel written in Bass

```python
import numpy as np
import jax
import jax.numpy as jnp

def _softmax(x, axis=-1):
    return jax.nn.softmax(x, axis=axis)

def _gelu(x):
    return jax.nn.gelu(x, approximate=True)

def _silu(x):
    return jax.nn.silu(x)

def _sigmoid(x):
    return jax.nn.sigmoid(x)

def _layernorm(x, axis=-1, eps=1e-05):
    m = jnp.mean(x, axis=axis, keepdims=True)
    v = jnp.var(x, axis=axis, keepdims=True)
    return (x - m) / jnp.sqrt(v + eps)

def _scatter_add(tgt, idx, src, axis=0):
    return tgt.at[idx].add(src)

def _segment_sum(src, seg, n):
    return jax.ops.segment_sum(src, seg, n)
kernel_name = 'mk_cond_resid_d2_seqx_r2_36115d'

def setup_inputs(seed: int=0):
    np.random.seed(seed)
    _w = jnp.asarray

    def _rec_inputs():
        import jax
        import jax.numpy as jnp
        _rk = jax.random.key(seed)
        x = -7.109e-05 + 0.9999 * jax.random.normal(jax.random.fold_in(_rk, 1), (32, 128, 1024), jnp.float32)
        _lenS = 128 - jax.random.randint(jax.random.fold_in(_rk, 7), (32,), 0, max(1, 128 // 4) + 1, jnp.int32)
        _lenS2 = 128 - jax.random.randint(jax.random.fold_in(_rk, 8), (32,), 0, max(1, 128 // 4) + 1, jnp.int32)
        itok_B_1_198 = jax.random.randint(jax.random.fold_in(_rk, 11), (32,), 1, 199, jnp.int32)
        cond_1 = jax.random.uniform(jax.random.fold_in(_rk, 12), (32, 1), jnp.float32, 0.0, 1.37214)
        return (x, itok_B_1_198, cond_1)
    x, itok_B_1_198, cond_1 = _rec_inputs()

    def _L0_cond_setup():
        import jax, jax.numpy as jnp
        import numpy as np
        B, C, T = (128, 128, 1024)
        S, D = (200, 128)
        key = jax.random.key(seed)
        k1, k2, k3 = jax.random.split(key, 3)
        x = jax.random.normal(k1, (B, C, T), dtype=jnp.float32)
        conditions = jax.random.randint(k2, (B,), 0, S, dtype=jnp.int64)
        weights = jax.random.normal(k3, (S, C, D), dtype=jnp.float32) / jnp.sqrt(jnp.float32(C))
        return {'x': x, 'conditions': conditions, 'weights': weights}
    _L0_cond_all = _L0_cond_setup()
    _L0_cond_in = {k: v for k, v in _L0_cond_all.items() if k in ('weights',)}
    del _L0_cond_all

    def _L1_cond_setup():
        import jax, jax.numpy as jnp
        import numpy as np
        B, S, D_MODEL, NHEAD = (4, 1024, 1024, 16)
        HEAD_DIM = D_MODEL // NHEAD
        key = jax.random.key(seed)
        ks = jax.random.split(key, 6)
        scale = 1.0 / np.sqrt(D_MODEL)
        return {'hidden_states': jax.random.normal(ks[0], (B, S, D_MODEL), dtype=jnp.float32), 'attention_precision': jax.random.uniform(ks[1], (B, 1, 1), dtype=jnp.float32, minval=0.5, maxval=2.0), 'Wq': jax.random.normal(ks[2], (D_MODEL, D_MODEL), dtype=jnp.float32) * scale, 'Wk': jax.random.normal(ks[3], (D_MODEL, D_MODEL), dtype=jnp.float32) * scale, 'Wv': jax.random.normal(ks[4], (D_MODEL, D_MODEL), dtype=jnp.float32) * scale, 'Wo': jax.random.normal(ks[5], (D_MODEL, D_MODEL), dtype=jnp.float32) * scale}
    _L1_cond_all = _L1_cond_setup()
    _L1_cond_in = {k: v for k, v in _L1_cond_all.items() if k in ('Wq', 'Wk', 'Wv', 'Wo')}
    del _L1_cond_all
    return {'x': x, 'itok_B_1_198': itok_B_1_198, 'cond_1': cond_1, 'L0_cond_weights': _L0_cond_in['weights'], 'L1_cond_Wq': _L1_cond_in['Wq'], 'L1_cond_Wk': _L1_cond_in['Wk'], 'L1_cond_Wv': _L1_cond_in['Wv'], 'L1_cond_Wo': _L1_cond_in['Wo']}

def reference(x, itok_B_1_198, cond_1, L0_cond_weights, L1_cond_Wq, L1_cond_Wk, L1_cond_Wv, L1_cond_Wo):
    import jax
    import jax.numpy as jnp

    def _L0_cond_ref(x, conditions, weights):
        import jax, jax.numpy as jnp
        import numpy as np
        B, C, T = (128, 128, 1024)
        S, D = (200, 128)
        w = weights[conditions]
        return jnp.einsum('bct,bcd->bdt', x, w)

    def _L1_cond_ref(hidden_states, attention_precision, Wq, Wk, Wv, Wo):
        import jax, jax.numpy as jnp
        import numpy as np
        B, S, D_MODEL, NHEAD = (4, 1024, 1024, 16)
        HEAD_DIM = D_MODEL // NHEAD
        b, s, _ = hidden_states.shape

        def proj(x, W):
            y = jnp.einsum('bsd,ed->bse', x, W)
            return y.reshape(b, s, NHEAD, HEAD_DIM).transpose(0, 2, 1, 3)
        q = proj(hidden_states, Wq)
        k = proj(hidden_states, Wk)
        v = proj(hidden_states, Wv)
        beta = jnp.minimum(attention_precision, 4.0)[:, None]
        q = q * beta
        scores = jnp.einsum('bhqd,bhkd->bhqk', q, k) / np.sqrt(HEAD_DIM)
        causal = jnp.tril(jnp.ones((s, s), dtype=bool))
        scores = jnp.where(causal, scores, jnp.finfo(scores.dtype).min)
        attn = jax.nn.softmax(scores, axis=-1)
        out = jnp.einsum('bhqk,bhkd->bhqd', attn, v)
        out = out.transpose(0, 2, 1, 3).reshape(b, s, D_MODEL)
        return jnp.einsum('bsd,ed->bse', out, Wo)
    x = x + _L0_cond_ref(x, itok_B_1_198, L0_cond_weights)
    x = x + _L1_cond_ref(x, cond_1[:, None, :], L1_cond_Wq, L1_cond_Wk, L1_cond_Wv, L1_cond_Wo)
    return x

_drawn_inputs = setup_inputs


def setup_inputs(seed=0):
    import zlib

    import numpy as np

    out = dict(_drawn_inputs(seed))
    spreads = {}
    factors = {}
    for name, (base, spread) in spreads.items():
        noise = np.random.default_rng([zlib.crc32(name.encode()), seed]).standard_normal(out[name].shape)
        drawn = base * np.exp(spread * noise) if base else spread * noise
        out[name] = jnp.asarray(drawn.astype(out[name].dtype))
    for name, factor in factors.items():
        out[name] = (out[name] * factor).astype(out[name].dtype)
    return out
```

```python
from contextlib import ExitStack

import numpy as np

import concourse.bass as bass
from concourse import mybir


B, S, D, H, HD = 32, 128, 1024, 16, 64
GB = 4
NG = B // GB
T = GB * S
DC = D // 128
NC = 4
NW = 200
NEG = -3.0e38


def cond_attention(nc, x, idx, cond, w0, wq, wk, wv, wo, mask_d, ident_d, out):
    f32, f32r, i32 = mybir.dt.float32, mybir.dt.float32r, mybir.dt.int32
    ACT, ALU, AX = mybir.ActivationFunctionType, mybir.AluOpType, mybir.AxisListType.X
    pe, act, dve, pool, sp = nc.tensor, nc.scalar, nc.vector, nc.gpsimd, nc.sync

    x1_d = nc.dram_tensor("x1_scratch", [B, 128, D], f32).ap()
    xt_d = nc.dram_tensor("xt_scratch", [NG, 128, DC * T], f32).ap()
    at_d = nc.dram_tensor("at_scratch", [NG, 128, DC * T], f32).ap()

    ctx = ExitStack()
    with ctx:
        def sb(name, shape, dt=f32):
            return ctx.enter_context(nc.sbuf_tensor("t_" + name, shape, dt))

        def pb(name):
            return ctx.enter_context(nc.psum_tensor("p_" + name, [128, 512], f32))

        def sem(name):
            return ctx.enter_context(nc.semaphore(name))

        WH = [sb(f"WH{n}", [128, DC, 512], f32r) for n in range(3)]
        WL = [sb(f"WL{n}", [128, DC, 512], f32r) for n in range(3)]
        XH = sb("XH", [128, DC, T], f32r)
        XL = sb("XL", [128, DC, T], f32r)
        XS = sb("XS", [128, DC, T])
        VH = sb("VH", [128, GB, 512], f32r)
        VL = sb("VL", [128, GB, 512], f32r)
        QH = sb("QH", [128, T], f32r)
        QL = sb("QL", [128, T], f32r)
        KH = sb("KH", [128, GB, 256], f32r)
        KL = sb("KL", [128, GB, 256], f32r)
        xr = sb("xr", [128, D])
        xh = sb("xh", [128, 512], f32r)
        xl = sb("xl", [128, 512], f32r)
        wr = sb("wr", [128, 128])
        wh = sb("wh", [128, 128], f32r)
        wl = sb("wl", [128, 128], f32r)
        WR = [sb(f"WR{n}", [128, 512]) for n in range(2)]
        SS = [sb(f"SS{n}", [128, 2, 128]) for n in range(2)]
        PP = [sb(f"PP{n}", [128, 2, 128]) for n in range(2)]
        PTH = [sb(f"PTH{n}", [128, 2, 128], f32r) for n in range(2)]
        PTL = [sb(f"PTL{n}", [128, 2, 128], f32r) for n in range(2)]
        AT = [sb(f"AT{n}", [128, T]) for n in range(2)]
        mask = sb("mask", [128, 128])
        ident = sb("ident", [128, 128])
        beta = sb("beta", [128, B])
        ix = sb("ix", [1, B], i32)
        ix2 = sb("ix2", [1, B], i32)
        st = sb("st", [128, 2, 8])

        PJ = [pb("PJ0"), pb("PJ1")]
        SC = [pb("SC0"), pb("SC1")]
        PT = [pb("PT0"), pb("PT1")]
        PV = pb("PV")
        LP = pb("LP")

        class Count:
            def __init__(self, name):
                self.sem, self.n = sem(name), 0

            def done(self, ins, by=1):
                ins.then_inc(self.sem, by)
                self.n += by
                return (self.sem, self.n)

        c_pe, c_act, c_dve = Count("pe_done"), Count("act_done"), Count("dve_done")
        waited = {}

        def wait(eng, *marks):
            for m in marks:
                if m is None:
                    continue
                key = (id(eng), id(m[0]))
                if waited.get(key, 0) < m[1]:
                    waited[key] = m[1]
                    eng.wait_ge(m[0], m[1])

        def PE(ins):
            return c_pe.done(ins)

        def A(ins):
            return c_act.done(ins)

        def V(ins):
            return c_dve.done(ins)

        l_x, l_w, l_xs = Count("load_x"), Count("load_w0"), Count("load_xs")
        l_xsb = [Count(f"load_xs_b{b}") for b in range(GB)]
        l_wr = [Count(f"load_wr{n}") for n in range(2)]
        l_c = [Count(f"load_c{n}") for n in range(4)]
        l_x1 = [Count(f"load_x1_{n}") for n in range(2)]
        s_x1, s_xt = Count("store_x1"), Count("store_xt")
        s_at = [Count(f"store_at{n}") for n in range(2)]
        s_out = [Count(f"store_out{n}") for n in range(2)]

        def split(dst_h, dst_l, src, src_ready, dst_free, before=None):
            wait(act, *src_ready, *dst_free)
            mh = A(act.activation(dst_h, src, ACT.Copy))
            wait(dve, *src_ready, *dst_free, mh)
            ml = V(dve.tensor_tensor(dst_l, src, dst_h.bitcast(f32), ALU.subtract))
            return mh, ml

        m_mask = l_c[0].done(sp.dma_start(mask[:], mask_d), 16)
        m_ident = l_c[1].done(sp.dma_start(ident[:], ident_d), 16)
        m_ix = l_c[2].done(sp.dma_start(ix[:], idx), 16)
        m_b = l_c[3].done(sp.dma_start(beta[:], cond.to_broadcast([128, B])), 16)
        wait(dve, m_ix)
        m = V(dve.tensor_scalar(ix2[:], ix[:], 0, NW, ALU.is_lt, ALU.mult))
        wait(dve, m)
        m = V(dve.tensor_tensor(ix[:], ix[:], ix2[:], ALU.add))
        wait(dve, m)
        m_ix = V(dve.tensor_scalar(ix2[:], ix[:], 0, NW - 1, ALU.max, ALU.min))
        wait(dve, m_b)
        m_beta = V(dve.tensor_scalar(beta[:], beta[:], 4.0, None, ALU.min))
        m_kz = V(dve.memset(KH[:].bitcast(f32), 0.0))
        m_kz = V(dve.memset(KL[:].bitcast(f32), 0.0))

        free_wr = [[], []]
        w_ready = [[None] * DC for _ in range(3)]
        w_free = [[] for _ in range(3)]
        n_wr = [0]

        def load_weight(slot, src, half, d):
            n = n_wr[0] % 2
            n_wr[0] += 1
            wait(sp, *free_wr[n])
            loaded = l_wr[n].done(sp.dma_start(WR[n][:], src[d * 128:(d + 1) * 128, half * 512:(half + 1) * 512]), 16)

            def finish():
                ms = split(WH[slot][:, d, :], WL[slot][:, d, :], WR[n][:], [loaded], w_free[slot])
                free_wr[n] = list(ms)
                w_ready[slot][d] = ms
            return finish

        todo = []
        place = [0]
        order = [0]

        def at(p, stage):
            order[0] += 1
            todo.append((max(p, place[0]), order[0], stage))

        def hook():
            place[0] += 1
            while True:
                ready = [t for t in todo if t[0] <= place[0]]
                if not ready:
                    return
                t = min(ready)
                todo.remove(t)
                t[2]()

        def weights_at(p, slot, src, half, every=2, lag=3):
            for d in range(DC):
                def start(d=d, p=p):
                    fin = load_weight(slot, src, half, d)
                    at(p + every * d + lag, fin)
                at(p + every * d, start)

        L = dict(x_free=[], w_free=[], h_free=[], lp_free=[])
        xs_free = []
        xs_ready = [[] for _ in range(GB)]

        def layer0(g, b, p, step=3):
            bb = g * GB + b
            box = {}

            def load():
                wait(sp, *L["x_free"])
                box["x"] = l_x.done(sp.dma_start(xr[:], x[bb]), 16)
                wait(sp, m_ix, *L["w_free"])
                r = sp.value_load(ix2[0:1, bb:bb + 1], min_val=0, max_val=NW - 1)
                box["w"] = l_w.done(sp.dma_start(wr[:], w0[bass.ds(r, 1), :, :].rearrange("o c d -> (o c) d")), 16)

            def split_w():
                box["ws"] = split(wh[:], wl[:], wr[:], [box["w"]], L["w_free"])
                box["x1"], box["st"], box["tp"] = [None, None], [None, None], [None, None]

            def half_a(h):
                c = slice(h * 512, (h + 1) * 512)
                box["xs"] = split(xh[:], xl[:], xr[:, c], [box["x"]], L["h_free"])
                wait(pe, *box["ws"], *box["xs"], *L["lp_free"])
                pe.matmul(LP[:], wh[:], xh[:], start=True, stop=False)
                pe.matmul(LP[:], wh[:], xl[:], start=False, stop=False)
                mm = PE(pe.matmul(LP[:], wl[:], xh[:], start=False, stop=True))
                L["h_free"] = [mm]
                wait(dve, mm)
                box["x1"][h] = V(dve.tensor_tensor(xr[:, c], LP[:], xr[:, c], ALU.add))
                L["lp_free"] = [box["x1"][h]]
                if h == 1:
                    L["w_free"] = [mm]
                    wait(sp, *box["x1"])
                    box["st"] = s_x1.done(sp.dma_start(x1_d[bb], xr[:]), 16)

            def half_b(h):
                wait(pe, box["x1"][h], m_ident)
                for k in range(4):
                    t = h * 4 + k
                    mm = pe.transpose(LP[:, k * 128:(k + 1) * 128], xr[:, t * 128:(t + 1) * 128], ident[:])
                mm = PE(mm)
                wait(act, mm, *xs_free)
                ev = A(act.activation(XS[:, h * 4:h * 4 + 4, b * 128:(b + 1) * 128],
                                      LP[:].rearrange("p (k s) -> p k s", k=4), ACT.Copy))
                L["lp_free"] = [ev]
                xs_ready[b].append(ev)
                if h == 1:
                    L["x_free"] = [mm, box["st"]]
                    if b == GB - 1:
                        wait(sp, *[m for r in xs_ready for m in r])
                        box["xt"] = s_xt.done(sp.dma_start(xt_d[g], XS[:].rearrange("p d t -> p (d t)")), 16)
                        st_xt.append(box["xt"])

            at(p, load)
            at(p + 2 * step, split_w)
            at(p + 2 * step, lambda: half_a(0))
            at(p + 3 * step, lambda: half_b(0))
            at(p + 4 * step, lambda: half_a(1))
            at(p + 5 * step, lambda: half_b(1))

        st_xt = []

        x_ready = [[None] * GB for _ in range(DC)]

        def split_xt(d, free):
            ready = [m for r in xs_ready for m in r]
            ms = split(XH[:, d, :], XL[:, d, :], XS[:, d, :], ready, free)
            for b in range(GB):
                x_ready[d][b] = ms
            return ms

        def reload_xs(src, g, marks, extra=()):
            wait(sp, *marks, *extra)
            m = l_xs.done(sp.dma_start(XS[:].rearrange("p d t -> p (d t)"), src[g]), 16)
            for b in range(GB):
                xs_ready[b][:] = [m]

        nblk = [0]
        pj_free = [[], []]

        def block(lhs, rhs, ready, per_chunk=None):
            n = nblk[0] % 2
            nblk[0] += 1
            wait(pe, *pj_free[n])
            for d in range(DC):
                wait(pe, *ready(d))
                (lh, ll), (rh, rl) = lhs(d), rhs(d)
                pe.matmul(PJ[n][:], lh, rh, start=(d == 0), stop=False)
                pe.matmul(PJ[n][:], lh, rl, start=False, stop=False)
                mm = pe.matmul(PJ[n][:], ll, rh, start=False, stop=(d == DC - 1))
                mark = None
                if per_chunk or d == DC - 1:
                    mark = PE(mm)
                if per_chunk:
                    per_chunk(d, mark)
                hook()
            return n, mark

        v_ready, v_free = [None] * GB, [[] for _ in range(GB)]
        q_ready, k_ready = [None], [None]
        q_free, k_free = [[]], [[]]

        def row_block(slot, b):
            cols = slice(b * 128, (b + 1) * 128)
            return block(lambda d: (XH[:, d, cols], XL[:, d, cols]),
                         lambda d: (WH[slot][:, d, :], WL[slot][:, d, :]),
                         lambda d: [*w_ready[slot][d], *x_ready[d][b]])

        def col_block(slot, c, per_chunk=None):
            cols = slice(c * 128, (c + 1) * 128)
            return block(lambda d: (WH[slot][:, d, cols], WL[slot][:, d, cols]),
                         lambda d: (XH[:, d, :], XL[:, d, :]),
                         lambda d: [*w_ready[slot][d], *[m for b in range(GB) for m in x_ready[d][b]]],
                         per_chunk)

        def v_block(b):
            n, mm = row_block(2, b)
            v_ready[b] = split(VH[:, b, :], VL[:, b, :], PJ[n][:], [mm], v_free[b])
            pj_free[n] = list(v_ready[b])
            w_free[2] = [mm]

        def q_block(g, c):
            n, mm = col_block(0, c)
            w_free[0] = [mm]
            wait(dve, mm, m_beta)
            pj = PJ[n][:].rearrange("p (b s) -> p b s", b=GB)
            sc = V(dve.tensor_tensor(pj, pj, beta[:, g * GB:(g + 1) * GB].unsqueeze(2).to_broadcast([128, GB, 128]), ALU.mult))
            q_ready[0] = split(QH[:], QL[:], PJ[n][:], [sc], q_free[0])
            pj_free[n] = list(q_ready[0])

        def k_block(c, per_chunk=None):
            n, mm = col_block(1, c, per_chunk)
            w_free[1] = [mm]
            pj = PJ[n][:].rearrange("p (b s) -> p b s", b=GB)
            ms = []
            for h in range(2):
                r, k = slice(64 * h, 64 * h + 64), slice(128 * h, 128 * h + 128)
                wait(act, mm, m_kz, *k_free[0])
                mh = A(act.activation(KH[r, :, k], pj[r], ACT.Copy))
                wait(dve, mh, mm, *k_free[0])
                ml = V(dve.tensor_tensor(KL[r, :, k], pj[r], KH[r, :, k].bitcast(f32), ALU.subtract))
                ms += [mh, ml]
            k_ready[0] = ms
            pj_free[n] = list(ms)

        sc_free, pt_free = [[], []], [[], []]
        pv_free = [[]]
        ss_free, pp_free, pth_free = [[], []], [[], []], [[], []]
        at_free = [[], []]
        n_at = [0]
        at_done = [[] for _ in range(NG)]

        def attention(g, ph, c, p0, places=(0, 2, 4, 6), lags=(3, 4, 6)):
            an = n_at[0] % 2
            n_at[0] += 1
            ev = []

            def unit(u):
                z, o = u % 2, (u % 2) * 256
                box = {}
                bank = SC[z]

                def scores():
                    cols = slice(u * 128, (u + 1) * 128)
                    wait(pe, *q_ready[0], *k_ready[0], *sc_free[z])
                    pe.matmul(bank[:, 0:256], QH[:, cols], KH[:, u, :], start=True, stop=False)
                    pe.matmul(bank[:, 0:256], QH[:, cols], KL[:, u, :], start=False, stop=False)
                    mm = PE(pe.matmul(bank[:, 0:256], QL[:, cols], KH[:, u, :], start=False, stop=True))
                    if u == GB - 1:
                        q_free[0], k_free[0] = [mm], [mm]
                    wait(dve, mm, m_mask, *ss_free[z])
                    ms = V(dve.scalar_tensor_tensor(
                        out=SS[z][:], in0=bank[:, 0:256].rearrange("p (h k) -> p h k", h=2), scalar=HD ** -0.5,
                        in1=mask[:].unsqueeze(1).to_broadcast([128, 2, 128]), op0=ALU.mult, op1=ALU.add))
                    sc_free[z] = [ms]
                    wait(dve, ms)
                    mx = V(dve.tensor_reduce(st[:, z, 0:2], SS[z][:], AX, ALU.max, negate=True))
                    wait(act, mx, *pp_free[z])
                    for h in range(2):
                        me = A(act.activation(PP[z][:, h, :], SS[z][:, h, :], ACT.Exp, bias=st[:, z, h:h + 1],
                                              scale=1.0, accum_out=st[:, z, 2 + h:3 + h]))
                    ss_free[z] = [me]
                    box["e"] = me

                def norm():
                    wait(dve, box["e"])
                    m = V(dve.reciprocal(st[:, z, 4:6], st[:, z, 2:4]))
                    wait(dve, m)
                    box["n"] = V(dve.tensor_tensor(PP[z][:], PP[z][:],
                                                   st[:, z, 4:6].unsqueeze(2).to_broadcast([128, 2, 128]), ALU.mult))

                def turn():
                    wait(pe, box["n"], m_ident, *pt_free[z])
                    pe.transpose(PT[z][:, 0:128], PP[z][:, 0, :], ident[:])
                    mm = PE(pe.transpose(PT[z][:, 128:256], PP[z][:, 1, :], ident[:]))
                    pp_free[z] = [mm]
                    pt = PT[z][:, 0:256].rearrange("p (h k) -> p h k", h=2)
                    box["p"] = split(PTH[z][:], PTL[z][:], pt, [mm], pth_free[z])
                    pt_free[z] = list(box["p"])

                def values():
                    cc = slice(c * 128, (c + 1) * 128)
                    wait(pe, *box["p"], *v_ready[u], *pv_free[0])
                    out_ = PV[:, o:o + 256]
                    pe.matmul(out_, VH[:, u, cc], PTH[z][:].rearrange("p h k -> p (h k)"), start=True, stop=False)
                    pe.matmul(out_, VH[:, u, cc], PTL[z][:].rearrange("p h k -> p (h k)"), start=False, stop=False)
                    mm = PE(pe.matmul(out_, VL[:, u, cc], PTH[z][:].rearrange("p h k -> p (h k)"), start=False, stop=True))
                    pth_free[z] = [mm]
                    v_free[u] = [mm]
                    if u % 2:
                        pv = PV[:].rearrange("p (u h k) -> p u h k", u=2, h=2)
                        dst = AT[an][:].rearrange("p (b s) -> p b s", b=GB)[:, u - 1:u + 1, :]
                        wait(act, mm, *at_free[an])
                        e0 = A(act.activation(dst[0:64], pv[0:64, :, 0, :], ACT.Copy))
                        wait(dve, mm, *at_free[an])
                        e1 = V(dve.tensor_copy(dst[64:128], pv[64:128, :, 1, :]))
                        ev.extend([e0, e1])
                        pv_free[0] = [e0, e1]
                    if u == GB - 1:
                        wait(sp, *ev)
                        j = ph * NC + c
                        m = s_at[an].done(sp.dma_start(at_d[g][:, j * T:(j + 1) * T], AT[an][:]), 16)
                        at_free[an] = [m]
                        at_done[g].append(m)

                p = p0 + places[u]
                at(p, scores)
                at(p + lags[0], norm)
                at(p + lags[1], turn)
                at(p + lags[2], values)

            for u in range(GB):
                unit(u)

        def run_until_empty(limit):
            while any(t[0] <= limit for t in todo):
                hook()

        for b in range(GB):
            layer0(0, b, b * 6, step=1)
        weights_at(1, 2, wv, 0)
        run_until_empty(40)
        for d in range(DC):
            split_xt(d, [])
        weights_at(place[0] + 1, 0, wq, 0)
        weights_at(place[0] + 17, 1, wk, 0)

        for ph in range(2):
            for g in range(NG):
                last = g == NG - 1
                base = place[0]
                if ph == 0 and not last:
                    xs_free = [m for d in range(DC) for m in x_ready[d][0]] + st_xt[-1:]
                    for b in range(GB):
                        xs_ready[b][:] = []
                        layer0(g + 1, b, base + 4 + 20 * b)
                elif ph == 0:
                    reload_xs(xt_d, 0, [m for d in range(DC) for m in x_ready[d][0]], st_xt)
                elif not last:
                    reload_xs(xt_d, g + 1, [m for d in range(DC) for m in x_ready[d][0]])
                else:
                    reload_xs(at_d, 0, [m for d in range(DC) for m in x_ready[d][0]], at_done[0])
                for b in range(GB):
                    v_block(b)
                if last:
                    if ph == 0:
                        weights_at(place[0] + 2, 2, wv, 1)
                    else:
                        weights_at(place[0] + 2, 2, wo, 0)
                for c in range(NC):
                    q_block(g, c)
                    if c == NC - 1 and last:
                        weights_at(place[0] + 2, 0, wq if ph == 0 else wo, 1)
                    k_block(c, (lambda d, m: split_xt(d, [m])) if c == NC - 1 else None)
                    attention(g, ph, c, place[0] + 2)
                if last and ph == 0:
                    weights_at(place[0] + 12, 1, wk, 1)

        OX = [xr, WR[0]]
        X1B = [VH, VL]
        ox_free = [[], []]
        ob_free = [[], []]
        xsb_free = [[] for _ in range(GB)]
        x1t = [sb_ for sb_ in (xr[:, 0:512], xr[:, 512:1024])]
        obt = [AT[0], AT[1]]
        x1_free = [L["x_free"], L["x_free"]]
        o_free = [at_free, at_free]
        n_out = [0]
        finals = []
        for b in range(GB):
            xs_ready[b][:] = []
        m_split0 = [m for d in range(DC) for m in x_ready[d][0]]

        def xs_batch(g, b, marks):
            wait(sp, *marks, *at_done[g])
            src = at_d[g].rearrange("p (d t) -> p d t", d=DC)[:, :, b * 128:(b + 1) * 128]
            m = l_xsb[b].done(sp.dma_start(XS[:, :, b * 128:(b + 1) * 128], src), 16)
            xs_ready[b][:] = [m]

        for b in range(GB):
            xs_batch(1, b, m_split0)
        for g in range(NG):
            for b in range(GB):
                bb = g * GB + b
                for half, slot in ((0, 2), (1, 0)):
                    i = n_out[0] % 2
                    n_out[0] += 1
                    wait(sp, *x1_free[i], (s_x1.sem, s_x1.n))
                    ld = l_x1[i].done(sp.dma_start(x1t[i], x1_d[bb][:, half * 512:(half + 1) * 512]), 16)
                    n, mm = row_block(slot, b)
                    o = obt[i]
                    wait(dve, mm, ld, *(ob_free[i] or at_free[i]))
                    ev = V(dve.tensor_tensor(o[:], PJ[n][:], x1t[i], ALU.add))
                    pj_free[n] = [ev]
                    x1_free[i] = [ev]
                    wait(sp, ev)
                    m = s_out[i].done(sp.dma_start(out[bb][:, half * 512:(half + 1) * 512], o[:]), 16)
                    ob_free[i] = [m]
                if g + 1 < NG:
                    ms = []
                    cols = slice(b * 128, (b + 1) * 128)
                    ms = split(XH[:, :, cols], XL[:, :, cols], XS[:, :, cols], xs_ready[b], [mm])
                    for d in range(DC):
                        x_ready[d][b] = ms
                    if g + 2 < NG:
                        xs_batch(g + 2, b, ms)
        for c in s_out + s_at + [s_x1, s_xt]:
            wait(sp, (c.sem, c.n))


_OUT = ((B, S, D), "float32")


def kernel(x, itok_B_1_198, cond_1, L0_cond_weights, L1_cond_Wq, L1_cond_Wk, L1_cond_Wv, L1_cond_Wo):
    import concourse.bacc as bacc
    from concourse.bass_utils import run_bass_kernel_spmd

    f = np.float32
    rows = np.arange(128)
    arrays = {
        "x": np.ascontiguousarray(x),
        "idx": np.ascontiguousarray(itok_B_1_198).reshape(1, B),
        "cond": np.ascontiguousarray(cond_1).reshape(1, B),
        "w0": np.ascontiguousarray(L0_cond_weights),
        "wq": np.ascontiguousarray(np.asarray(L1_cond_Wq).T),
        "wk": np.ascontiguousarray(np.asarray(L1_cond_Wk).T),
        "wv": np.ascontiguousarray(np.asarray(L1_cond_Wv).T),
        "wo": np.ascontiguousarray(np.asarray(L1_cond_Wo).T),
        "mask": np.where(rows[None, :] <= rows[:, None], f(0), f(NEG)).astype(f),
        "ident": np.eye(128, dtype=f),
    }
    nc = bacc.Bacc("TRN2", target_bir_lowering=False, num_devices=1)
    args = [nc.dram_tensor(n, a.shape, mybir.dt.from_np(a.dtype), kind="ExternalInput").ap() for n, a in arrays.items()]
    out = nc.dram_tensor("out", _OUT[0], mybir.dt.from_np(np.dtype(_OUT[1])), kind="ExternalOutput").ap()
    cond_attention(nc, *args, out)
    r = run_bass_kernel_spmd(nc, [arrays], core_ids=[0])
    return r.results[0]["out"]
```

```python
from contextlib import ExitStack

import numpy as np

import concourse.bass as bass
from concourse import mybir


B, S, D, H, HD = 32, 128, 1024, 16, 64
GB = 4
NG = B // GB
T = GB * S
DC = D // 128
NC = 4
NW = 200
NEG = -3.0e38


def cond_attention(nc, x, idx, cond, w0, wq, wk, wv, wo, mask_d, ident_d, out):
    f32, f32r, i32 = mybir.dt.float32, mybir.dt.float32r, mybir.dt.int32
    ACT, ALU, AX = mybir.ActivationFunctionType, mybir.AluOpType, mybir.AxisListType.X
    pe, act, dve, pool, sp = nc.tensor, nc.scalar, nc.vector, nc.gpsimd, nc.sync

    x1_d = nc.dram_tensor("x1_scratch", [B, 128, D], f32).ap()
    xt_d = nc.dram_tensor("xt_scratch", [NG, 128, DC * T], f32).ap()
    at_d = nc.dram_tensor("at_scratch", [NG, 128, DC * T], f32).ap()

    ctx = ExitStack()
    with ctx:
        def sb(name, shape, dt=f32):
            return ctx.enter_context(nc.sbuf_tensor("t_" + name, shape, dt))

        def pb(name):
            return ctx.enter_context(nc.psum_tensor("p_" + name, [128, 512], f32))

        def sem(name):
            return ctx.enter_context(nc.semaphore(name))

        WH = [sb(f"WH{n}", [128, DC, 512], f32r) for n in range(3)]
        WL = [sb(f"WL{n}", [128, DC, 512], f32r) for n in range(3)]
        XH = sb("XH", [128, DC, T], f32r)
        XL = sb("XL", [128, DC, T], f32r)
        XS = sb("XS", [128, DC, T])
        VH = sb("VH", [128, GB, 512], f32r)
        VL = sb("VL", [128, GB, 512], f32r)
        QH = sb("QH", [128, T], f32r)
        QL = sb("QL", [128, T], f32r)
        KH = sb("KH", [128, GB, 256], f32r)
        KL = sb("KL", [128, GB, 256], f32r)
        xr = [sb(f"xr{n}", [128, D]) for n in range(2)]
        xh = sb("xh", [128, 512], f32r)
        xl = sb("xl", [128, 512], f32r)
        wr = [sb(f"wr{n}", [128, 128]) for n in range(2)]
        wh = sb("wh", [128, 128], f32r)
        wl = sb("wl", [128, 128], f32r)
        WR = [sb(f"WR{n}", [128, 512]) for n in range(3)]
        SS = [sb(f"SS{n}", [128, 2, 128]) for n in range(2)]
        PP = [sb(f"PP{n}", [128, 2, 128]) for n in range(4)]
        PTH = [sb(f"PTH{n}", [128, 2, 128], f32r) for n in range(2)]
        PTL = [sb(f"PTL{n}", [128, 2, 128], f32r) for n in range(2)]
        AT = [sb(f"AT{n}", [128, T]) for n in range(2)]
        mask = sb("mask", [128, 128])
        ident = sb("ident", [128, 128])
        beta = sb("beta", [128, B])
        ix = sb("ix", [1, B], i32)
        ix2 = sb("ix2", [1, B], i32)
        st = sb("st", [128, GB, 8])

        PJ = [pb("PJ0"), pb("PJ1")]
        SC = [pb("SC0"), pb("SC1")]
        PT = [pb("PT0"), pb("PT1")]
        PV = pb("PV")
        LP = pb("LP")

        class Count:
            def __init__(self, name):
                self.sem, self.n = sem(name), 0

            def done(self, ins, by=1):
                ins.then_inc(self.sem, by)
                self.n += by
                return (self.sem, self.n)

        c_pe, c_act, c_dve = Count("pe_done"), Count("act_done"), Count("dve_done")
        waited = {}

        def wait(eng, *marks):
            for m in marks:
                if m is None:
                    continue
                key = (id(eng), id(m[0]))
                if waited.get(key, 0) < m[1]:
                    waited[key] = m[1]
                    eng.wait_ge(m[0], m[1])

        def PE(ins):
            return c_pe.done(ins)

        def A(ins):
            return c_act.done(ins)

        def V(ins):
            return c_dve.done(ins)

        l_xs = Count("load_xs")
        l_x = [Count(f"load_x{n}") for n in range(2)]
        l_w = [Count(f"load_w{n}") for n in range(2)]
        l_xsb = [Count(f"load_xs_b{b}") for b in range(GB)]
        l_wr = [Count(f"load_wr{n}") for n in range(3)]
        l_c = [Count(f"load_c{n}") for n in range(4)]
        l_x1 = [Count(f"load_x1_{n}") for n in range(2)]
        s_xt = Count("store_xt")
        s_x1 = [Count(f"store_x1_{n}") for n in range(2)]
        s_at = [Count(f"store_at{n}") for n in range(2)]
        s_out = [Count(f"store_out{n}") for n in range(2)]

        def split(dst_h, dst_l, src, src_ready, dst_free, later=1):
            free = list(dst_free)
            wait(act, *src_ready, *free)
            ms = [A(act.activation(dst_h, src, ACT.Copy))]

            def low():
                wait(dve, *src_ready, *free, ms[0])
                ms.append(V(dve.tensor_tensor(dst_l, src, dst_h.bitcast(f32), ALU.subtract)))
            if later:
                at(place[0] + later, low)
            else:
                low()
            return ms

        m_mask = l_c[0].done(sp.dma_start(mask[:], mask_d), 16)
        m_ident = l_c[1].done(sp.dma_start(ident[:], ident_d), 16)
        m_ix = l_c[2].done(sp.dma_start(ix[:], idx), 16)
        m_b = l_c[3].done(sp.dma_start(beta[:], cond.to_broadcast([128, B])), 16)
        wait(dve, m_ix)
        m = V(dve.tensor_scalar(ix2[:], ix[:], 0, NW, ALU.is_lt, ALU.mult))
        wait(dve, m)
        m = V(dve.tensor_tensor(ix[:], ix[:], ix2[:], ALU.add))
        wait(dve, m)
        m_ix = V(dve.tensor_scalar(ix2[:], ix[:], 0, NW - 1, ALU.max, ALU.min))
        wait(dve, m_b)
        m_beta = V(dve.tensor_scalar(beta[:], beta[:], 4.0, None, ALU.min))
        m_kz = V(dve.memset(KH[:].bitcast(f32), 0.0))
        m_kz = V(dve.memset(KL[:].bitcast(f32), 0.0))

        free_wr = [[], [], []]
        w_ready = [[None] * DC for _ in range(3)]
        w_free = [[] for _ in range(3)]
        n_wr = [0]

        def load_weight(slot, src, half, d):
            n = n_wr[0] % 3
            n_wr[0] += 1
            wait(sp, *free_wr[n])
            loaded = l_wr[n].done(sp.dma_start(WR[n][:], src[d * 128:(d + 1) * 128, half * 512:(half + 1) * 512]), 16)

            def finish():
                ms = split(WH[slot][:, d, :], WL[slot][:, d, :], WR[n][:], [loaded], w_free[slot])
                free_wr[n] = ms
                w_ready[slot][d] = ms
            return finish

        todo = []
        place = [0]
        order = [0]

        def at(p, stage):
            order[0] += 1
            todo.append((max(p, place[0]), order[0], stage))

        def hook():
            place[0] += 1
            while True:
                ready = [t for t in todo if t[0] <= place[0]]
                if not ready:
                    return
                t = min(ready)
                todo.remove(t)
                t[2]()

        def weights_at(p, slot, src, half, every=2, lag=3):
            for d in range(DC):
                def start(d=d, p=p):
                    fin = load_weight(slot, src, half, d)
                    at(p + every * d + lag, fin)
                at(p + every * d, start)

        x_free, w0_free = [[], []], [[], []]
        h_free, wh_free, lp_free = [[]], [[]], [[]]
        xs_free = [[] for _ in range(GB)]
        xs_ready = [[] for _ in range(GB)]

        def layer0(g, b, load_p, p, offsets=(3, 4, 6, 8, 11)):
            bb, z = g * GB + b, b % 2
            xb, wb = xr[z], wr[z]
            box = {"x1": [None, None]}

            def load():
                wait(sp, *x_free[z])
                box["x"] = l_x[z].done(sp.dma_start(xb[:], x[bb]), 16)
                wait(sp, m_ix, *w0_free[z])
                r = sp.value_load(ix2[0:1, bb:bb + 1], min_val=0, max_val=NW - 1)
                box["w"] = l_w[z].done(sp.dma_start(wb[:], w0[bass.ds(r, 1), :, :].rearrange("o c d -> (o c) d")), 16)

            def split_w():
                box["ws"] = split(wh[:], wl[:], wb[:], [box["w"]], wh_free[0])
                w0_free[z] = box["ws"]
                split_x(0)

            def split_x(h):
                box["xs"] = split(xh[:], xl[:], xb[:, h * 512:(h + 1) * 512], [box["x"]], h_free[0])

            def half_a(h):
                c = slice(h * 512, (h + 1) * 512)
                wait(pe, *box["ws"], *box["xs"], *lp_free[0])
                pe.matmul(LP[:], wh[:], xh[:], start=True, stop=False)
                pe.matmul(LP[:], wh[:], xl[:], start=False, stop=False)
                mm = PE(pe.matmul(LP[:], wl[:], xh[:], start=False, stop=True))
                h_free[0] = [mm]
                wait(dve, mm)
                box["x1"][h] = V(dve.tensor_tensor(xb[:, c], LP[:], xb[:, c], ALU.add))
                lp_free[0] = [box["x1"][h]]
                if h == 1:
                    wh_free[0] = [mm]
                    wait(sp, *box["x1"])
                    box["st"] = s_x1[z].done(sp.dma_start(x1_d[bb], xb[:]), 16)

            def half_b(h):
                wait(pe, box["x1"][h], m_ident)
                for k in range(4):
                    t = h * 4 + k
                    mm = pe.transpose(LP[:, k * 128:(k + 1) * 128], xb[:, t * 128:(t + 1) * 128], ident[:])
                mm = PE(mm)
                wait(act, mm, *xs_free[b])
                ev = A(act.activation(XS[:, h * 4:h * 4 + 4, b * 128:(b + 1) * 128],
                                      LP[:].rearrange("p (k s) -> p k s", k=4), ACT.Copy))
                lp_free[0] = [ev]
                xs_ready[b].append(ev)
                if h == 1:
                    x_free[z] = [mm, box["st"]]
                    if b == GB - 1:
                        wait(sp, *[m for r in xs_ready for m in r])
                        st_xt.append(s_xt.done(sp.dma_start(xt_d[g], XS[:].rearrange("p d t -> p (d t)")), 16))

            at(load_p, load)
            at(p, split_w)
            at(p + offsets[0], lambda: half_a(0))
            at(p + offsets[1], lambda: split_x(1))
            at(p + offsets[2], lambda: half_b(0))
            at(p + offsets[3], lambda: half_a(1))
            at(p + offsets[4], lambda: half_b(1))

        st_xt = []

        x_ready = [[None] * GB for _ in range(DC)]

        def split_xt(d, free):
            ready = [m for r in xs_ready for m in r]
            ms = split(XH[:, d, :], XL[:, d, :], XS[:, d, :], ready, free)
            for b in range(GB):
                x_ready[d][b] = ms
            return ms

        def split_xt_batch(b, free, later=1):
            cols = slice(b * 128, (b + 1) * 128)
            ms = split(XH[:, :, cols], XL[:, :, cols], XS[:, :, cols], xs_ready[b], free, later)
            for d in range(DC):
                x_ready[d][b] = ms
            return ms

        def reload_xs(src, g, marks, extra=()):
            wait(sp, *marks, *extra)
            m = l_xs.done(sp.dma_start(XS[:].rearrange("p d t -> p (d t)"), src[g]), 16)
            for b in range(GB):
                xs_ready[b][:] = [m]

        nblk = [0]
        pj_free = [[], []]

        def block(lhs, rhs, ready):
            n = nblk[0] % 2
            nblk[0] += 1
            wait(pe, *pj_free[n])
            for d in range(DC):
                wait(pe, *ready(d))
                (lh, ll), (rh, rl) = lhs(d), rhs(d)
                pe.matmul(PJ[n][:], lh, rh, start=(d == 0), stop=False)
                pe.matmul(PJ[n][:], lh, rl, start=False, stop=False)
                mm = pe.matmul(PJ[n][:], ll, rh, start=False, stop=(d == DC - 1))
                if d == DC - 1:
                    mm = PE(mm)
                hook()
            return n, mm

        v_ready, v_free = [None] * GB, [[] for _ in range(GB)]
        q_ready, k_ready = [None], [None]
        q_free, k_free = [[]], [[]]

        def row_block(slot, b):
            cols = slice(b * 128, (b + 1) * 128)
            return block(lambda d: (XH[:, d, cols], XL[:, d, cols]),
                         lambda d: (WH[slot][:, d, :], WL[slot][:, d, :]),
                         lambda d: [*w_ready[slot][d], *x_ready[d][b]])

        def col_block(slot, c):
            cols = slice(c * 128, (c + 1) * 128)
            return block(lambda d: (WH[slot][:, d, cols], WL[slot][:, d, cols]),
                         lambda d: (XH[:, d, :], XL[:, d, :]),
                         lambda d: [*w_ready[slot][d], *[m for b in range(GB) for m in x_ready[d][b]]])

        def v_block(b, later):
            n, mm = row_block(2, b)
            w_free[2] = [mm]

            def empty():
                v_ready[b] = split(VH[:, b, :], VL[:, b, :], PJ[n][:], [mm], v_free[b])
                pj_free[n] = v_ready[b]
            if later:
                at(place[0] + later, empty)
            else:
                empty()

        def q_empty(g, n, mm):
            w_free[0] = [mm]
            wait(dve, mm, m_beta)
            pj = PJ[n][:].rearrange("p (b s) -> p b s", b=GB)
            sc = V(dve.tensor_tensor(pj, pj, beta[:, g * GB:(g + 1) * GB].unsqueeze(2).to_broadcast([128, GB, 128]), ALU.mult))
            q_ready[0] = split(QH[:], QL[:], PJ[n][:], [sc], q_free[0])
            pj_free[n] = q_ready[0]

        def k_empty(n, mm):
            w_free[1] = [mm]
            pj = PJ[n][:].rearrange("p (b s) -> p b s", b=GB)
            free = list(k_free[0])
            wait(act, mm, m_kz, *free)
            parts = [(slice(64 * h, 64 * h + 64), slice(128 * h, 128 * h + 128)) for h in range(2)]
            ms = [A(act.activation(KH[r, :, k], pj[r], ACT.Copy)) for r, k in parts]

            def low():
                wait(dve, mm, *free)
                for h, (r, k) in enumerate(parts):
                    wait(dve, ms[h])
                    ms.append(V(dve.tensor_tensor(KL[r, :, k], pj[r], KH[r, :, k].bitcast(f32), ALU.subtract)))
            at(place[0] + 1, low)
            k_ready[0] = ms
            pj_free[n] = ms

        def last_blocks(g, c):
            banks = [nblk[0] % 2, (nblk[0] + 1) % 2]
            nblk[0] += 2
            cols = slice(c * 128, (c + 1) * 128)

            def step(slot, d):
                n = banks[slot]
                if d == 0:
                    wait(pe, *pj_free[n])
                wait(pe, *w_ready[slot][d], *[m for b in range(GB) for m in x_ready[d][b]])
                lh, ll, rh, rl = WH[slot][:, d, cols], WL[slot][:, d, cols], XH[:, d, :], XL[:, d, :]
                pe.matmul(PJ[n][:], lh, rh, start=(d == 0), stop=False)
                pe.matmul(PJ[n][:], lh, rl, start=False, stop=False)
                mm = pe.matmul(PJ[n][:], ll, rh, start=False, stop=(d == DC - 1))
                if slot == 1:
                    mm = PE(mm)
                    split_xt(d, [mm])
                elif d == DC - 1:
                    mm = PE(mm)
                hook()
                return mm

            for i in range(DC + 2):
                if i < DC:
                    mm = step(0, i)
                    if i == DC - 1:
                        q_empty(g, banks[0], mm)
                if i >= 2:
                    mm = step(1, i - 2)
            k_empty(banks[1], mm)

        sc_free, pt_free = [[], []], [[], []]
        pv_free = [[]]
        ss_free, pp_free, pth_free = [[], []], [[] for _ in range(GB)], [[], []]
        at_free = [[], []]
        n_at = [0]
        at_done = [[] for _ in range(NG)]

        def attention(g, ph, c, p0, places=(0, 2, 4, 5), lags=(2, 4, 5, 8)):
            an = n_at[0] % 2
            n_at[0] += 1
            ev = []

            def unit(u):
                z, o = u % 2, (u % 2) * 256
                box = {}
                bank = SC[z]

                def scores():
                    cols = slice(u * 128, (u + 1) * 128)
                    wait(pe, *q_ready[0], *k_ready[0], *sc_free[z])
                    pe.matmul(bank[:, 0:256], QH[:, cols], KH[:, u, :], start=True, stop=False)
                    pe.matmul(bank[:, 0:256], QH[:, cols], KL[:, u, :], start=False, stop=False)
                    mm = PE(pe.matmul(bank[:, 0:256], QL[:, cols], KH[:, u, :], start=False, stop=True))
                    if u == GB - 1:
                        q_free[0], k_free[0] = [mm], [mm]
                    wait(dve, mm, m_mask, *ss_free[z])
                    ms = V(dve.scalar_tensor_tensor(
                        out=SS[z][:], in0=bank[:, 0:256].rearrange("p (h k) -> p h k", h=2), scalar=HD ** -0.5,
                        in1=mask[:].unsqueeze(1).to_broadcast([128, 2, 128]), op0=ALU.mult, op1=ALU.add))
                    sc_free[z] = [ms]
                    wait(dve, ms)
                    mx = V(dve.tensor_reduce(st[:, u, 0:2], SS[z][:], AX, ALU.max, negate=True))
                    box["mx"] = mx

                def exps():
                    wait(act, box["mx"], *pp_free[u])
                    for h in range(2):
                        me = A(act.activation(PP[u][:, h, :], SS[z][:, h, :], ACT.Exp, bias=st[:, u, h:h + 1],
                                              scale=1.0, accum_out=st[:, u, 2 + h:3 + h]))
                    ss_free[z] = [me]
                    box["e"] = me

                def norm():
                    wait(dve, box["e"])
                    m = V(dve.reciprocal(st[:, u, 4:6], st[:, u, 2:4]))
                    wait(dve, m)
                    box["n"] = V(dve.tensor_tensor(PP[u][:], PP[u][:],
                                                   st[:, u, 4:6].unsqueeze(2).to_broadcast([128, 2, 128]), ALU.mult))

                def turn():
                    wait(pe, box["n"], m_ident, *pt_free[z])
                    pe.transpose(PT[z][:, 0:128], PP[u][:, 0, :], ident[:])
                    mm = PE(pe.transpose(PT[z][:, 128:256], PP[u][:, 1, :], ident[:]))
                    pp_free[u] = [mm]
                    pt = PT[z][:, 0:256].rearrange("p (h k) -> p h k", h=2)
                    box["p"] = split(PTH[z][:], PTL[z][:], pt, [mm], pth_free[z])
                    pt_free[z] = box["p"]

                def values():
                    cc = slice(c * 128, (c + 1) * 128)
                    wait(pe, *box["p"], *v_ready[u], *pv_free[0])
                    out_ = PV[:, o:o + 256]
                    pe.matmul(out_, VH[:, u, cc], PTH[z][:].rearrange("p h k -> p (h k)"), start=True, stop=False)
                    pe.matmul(out_, VH[:, u, cc], PTL[z][:].rearrange("p h k -> p (h k)"), start=False, stop=False)
                    mm = PE(pe.matmul(out_, VL[:, u, cc], PTH[z][:].rearrange("p h k -> p (h k)"), start=False, stop=True))
                    pth_free[z] = [mm]
                    v_free[u] = [mm]
                    if u % 2:
                        pv = PV[:].rearrange("p (u h k) -> p u h k", u=2, h=2)
                        dst = AT[an][:].rearrange("p (b s) -> p b s", b=GB)[:, u - 1:u + 1, :]
                        wait(act, mm, *at_free[an])
                        e0 = A(act.activation(dst[0:64], pv[0:64, :, 0, :], ACT.Copy))
                        wait(dve, mm, *at_free[an])
                        e1 = V(dve.tensor_copy(dst[64:128], pv[64:128, :, 1, :]))
                        ev.extend([e0, e1])
                        pv_free[0] = [e0, e1]
                    if u == GB - 1:
                        wait(sp, *ev)
                        j = ph * NC + c
                        m = s_at[an].done(sp.dma_start(at_d[g][:, j * T:(j + 1) * T], AT[an][:]), 16)
                        at_free[an] = [m]
                        at_done[g].append(m)

                p = p0 + places[u]
                at(p, scores)
                at(p + lags[0], exps)
                at(p + lags[1], norm)
                at(p + lags[2], turn)
                at(p + lags[3], values)

            for u in range(GB):
                unit(u)

        FIRST = 8
        layer0(0, 0, 0, 1, offsets=(2, 3, 4, 6, 7))
        weights_at(1, 2, wv, 0, every=1, lag=1)
        for b in range(1, GB):
            layer0(0, b, 1 if b == 1 else 8 * b, FIRST + 8 * b - 8, offsets=(2, 3, 4, 6, 8))
        weights_at(FIRST + 4, 0, wq, 0)
        weights_at(FIRST + 21, 1, wk, 0)
        while place[0] < FIRST:
            hook()

        for ph in range(2):
            for g in range(NG):
                first, last = ph == 0 and g == 0, g == NG - 1
                base = place[0]
                xs_read = [m for d in range(DC) for m in (x_ready[d][0] or ())]
                if ph == 0 and not last:
                    if not first:
                        for b in range(GB):
                            xs_free[b] = xs_read + st_xt[-1:]
                            xs_ready[b][:] = []
                            layer0(g + 1, b, base + 2 + 18 * b, base + 8 + 18 * b)
                elif ph == 0:
                    reload_xs(xt_d, 0, xs_read, st_xt)
                elif not last:
                    reload_xs(xt_d, g + 1, xs_read)
                else:
                    reload_xs(at_d, 0, xs_read, at_done[0])
                for b in range(GB):
                    if first:
                        xs_free[b] = split_xt_batch(b, [], later=0)
                    v_block(b, 4 if b == 0 and not first else 0)
                if first:
                    for b in range(GB):
                        xs_free[b] = [*xs_free[b], *st_xt]
                        xs_ready[b][:] = []
                        layer0(1, b, place[0] + 1 + 12 * b, place[0] + 3 + 12 * b, offsets=(3, 4, 6, 8, 10))
                if last:
                    weights_at(place[0] + 2, 2, *((wv, 1) if ph == 0 else (wo, 0)))
                for c in range(NC - 1):
                    n, mm = col_block(0, c)
                    q_empty(g, n, mm)
                    n, mm = col_block(1, c)
                    k_empty(n, mm)
                    attention(g, ph, c, place[0] + 3)
                last_blocks(g, NC - 1)
                attention(g, ph, NC - 1, place[0] + 3)
                if last:
                    weights_at(place[0] + 2, 0, *((wq, 1) if ph == 0 else (wo, 1)))
                if last and ph == 0:
                    weights_at(place[0] + 18, 1, wk, 1)

        x1_free = [x_free[0], x_free[1]]
        o_free = [[], []]
        n_out = 0
        xs_read = [m for d in range(DC) for m in x_ready[d][0]]
        stored_x1 = [(c.sem, c.n) for c in s_x1]

        def xs_batch(g, b, marks):
            wait(sp, *marks, *at_done[g])
            cols = slice(b * 128, (b + 1) * 128)
            src = at_d[g].rearrange("p (d t) -> p d t", d=DC)[:, :, cols]
            xs_ready[b][:] = [l_xsb[b].done(sp.dma_start(XS[:, :, cols], src), 16)]

        for b in range(GB):
            xs_batch(1, b, xs_read)
        for g in range(NG):
            turns = [(b, h) for b in range(GB) for h in range(2)]
            if g == 0:
                turns.sort(key=lambda t: t[1])
            for b, half in turns:
                bb, slot = g * GB + b, (2, 0)[half]
                i = n_out % 2
                n_out += 1
                cols = slice(half * 512, (half + 1) * 512)
                wait(sp, *x1_free[i], *stored_x1)
                loaded = l_x1[i].done(sp.dma_start(xr[i][:, 0:512], x1_d[bb][:, cols]), 16)
                n, mm = row_block(slot, b)
                wait(dve, mm, loaded, *(o_free[i] or at_free[i]))
                ev = V(dve.tensor_tensor(AT[i][:], PJ[n][:], xr[i][:, 0:512], ALU.add))
                pj_free[n], x1_free[i] = [ev], [ev]
                wait(sp, ev)
                o_free[i] = [s_out[i].done(sp.dma_start(out[bb][:, cols], AT[i][:]), 16)]
                if half == 1 and g + 1 < NG:
                    ms = split_xt_batch(b, [mm])
                    if g + 2 < NG:
                        at(place[0] + 2, lambda g=g, b=b, ms=ms: xs_batch(g + 2, b, ms))
        for c in [*s_out, *s_at, *s_x1, s_xt]:
            wait(sp, (c.sem, c.n))


_OUT = ((B, S, D), "float32")


def kernel(x, itok_B_1_198, cond_1, L0_cond_weights, L1_cond_Wq, L1_cond_Wk, L1_cond_Wv, L1_cond_Wo):
    import concourse.bacc as bacc
    from concourse.bass_utils import run_bass_kernel_spmd

    f = np.float32
    rows = np.arange(128)
    arrays = {
        "x": np.ascontiguousarray(x),
        "idx": np.ascontiguousarray(itok_B_1_198).reshape(1, B),
        "cond": np.ascontiguousarray(cond_1).reshape(1, B),
        "w0": np.ascontiguousarray(L0_cond_weights),
        "wq": np.ascontiguousarray(np.asarray(L1_cond_Wq).T),
        "wk": np.ascontiguousarray(np.asarray(L1_cond_Wk).T),
        "wv": np.ascontiguousarray(np.asarray(L1_cond_Wv).T),
        "wo": np.ascontiguousarray(np.asarray(L1_cond_Wo).T),
        "mask": np.where(rows[None, :] <= rows[:, None], f(0), f(NEG)).astype(f),
        "ident": np.eye(128, dtype=f),
    }
    nc = bacc.Bacc("TRN2", target_bir_lowering=False, num_devices=1)
    args = [nc.dram_tensor(n, a.shape, mybir.dt.from_np(a.dtype), kind="ExternalInput").ap() for n, a in arrays.items()]
    out = nc.dram_tensor("out", _OUT[0], mybir.dt.from_np(np.dtype(_OUT[1])), kind="ExternalOutput").ap()
    cond_attention(nc, *args, out)
    r = run_bass_kernel_spmd(nc, [arrays], core_ids=[0])
    return r.results[0]["out"]
```

```python
from contextlib import ExitStack

import numpy as np

import concourse.bass as bass
from concourse import mybir


B, S, D, H, HD = 32, 128, 1024, 16, 64
GB = 4
NG = B // GB
T = GB * S
DC = D // 128
NC = 4
NW = 200
NEG = -3.0e38
Q_LATER = 5


def cond_attention(nc, x, idx, cond, w0, wq, wk, wv, wo, mask_d, ident_d, out):
    f32, f32r, i32 = mybir.dt.float32, mybir.dt.float32r, mybir.dt.int32
    ACT, ALU, AX = mybir.ActivationFunctionType, mybir.AluOpType, mybir.AxisListType.X
    pe, act, dve, pool, sp = nc.tensor, nc.scalar, nc.vector, nc.gpsimd, nc.sync

    x1_d = nc.dram_tensor("x1_scratch", [B, 128, D], f32).ap()
    xt_d = nc.dram_tensor("xt_scratch", [NG, 128, DC * T], f32).ap()
    at_d = nc.dram_tensor("at_scratch", [NG, 128, DC * T], f32).ap()

    ctx = ExitStack()
    with ctx:
        def sb(name, shape, dt=f32):
            return ctx.enter_context(nc.sbuf_tensor("t_" + name, shape, dt))

        def pb(name):
            return ctx.enter_context(nc.psum_tensor("p_" + name, [128, 512], f32))

        def sem(name):
            return ctx.enter_context(nc.semaphore(name))

        WH = [sb(f"WH{n}", [128, DC, 512], f32r) for n in range(3)]
        WL = [sb(f"WL{n}", [128, DC, 512], f32r) for n in range(3)]
        XH = sb("XH", [128, DC, T], f32r)
        XL = sb("XL", [128, DC, T], f32r)
        XS = sb("XS", [128, DC, T])
        VH = sb("VH", [128, GB, 512], f32r)
        VL = sb("VL", [128, GB, 512], f32r)
        QH = sb("QH", [128, T], f32r)
        QL = sb("QL", [128, T], f32r)
        KH = sb("KH", [128, GB, 256], f32r)
        KL = sb("KL", [128, GB, 256], f32r)
        xr = [sb(f"xr{n}", [128, D]) for n in range(2)]
        xh = sb("xh", [128, 512], f32r)
        xl = sb("xl", [128, 512], f32r)
        wr = [sb(f"wr{n}", [128, 128]) for n in range(2)]
        wh = sb("wh", [128, 128], f32r)
        wl = sb("wl", [128, 128], f32r)
        WR = [sb(f"WR{n}", [128, 512]) for n in range(3)]
        TP = sb("TP", [128, 2, 2, 128])
        PPT = sb("PP", [128, GB, 2, 128])
        PP = [PPT[:, u] for u in range(GB)]
        PTH = [sb(f"PTH{n}", [128, 2, 128], f32r) for n in range(2)]
        PTL = [sb(f"PTL{n}", [128, 2, 128], f32r) for n in range(2)]
        AT = [sb(f"AT{n}", [128, T]) for n in range(2)]
        mask = sb("mask", [128, 128])
        ident = sb("ident", [128, 128])
        beta = sb("beta", [128, B])
        ix = sb("ix", [1, B], i32)
        ix2 = sb("ix2", [1, B], i32)
        st = sb("st", [128, GB, 8])

        PJ = [pb(f"PJ{n}") for n in range(3)]
        SC = [pb("SC0"), pb("SC1")]
        PV = [pb("PV0"), pb("PV1")]
        LP = pb("LP")

        class Count:
            def __init__(self, name):
                self.sem, self.n = sem(name), 0

            def done(self, ins, by=1):
                ins.then_inc(self.sem, by)
                self.n += by
                return (self.sem, self.n)

        c_pe, c_act, c_dve, c_pool = (Count(f"{e}_done") for e in ("pe", "act", "dve", "pool"))
        waited = {}

        def wait(eng, *marks):
            for m in marks:
                if m is None:
                    continue
                key = (id(eng), id(m[0]))
                if waited.get(key, 0) < m[1]:
                    waited[key] = m[1]
                    eng.wait_ge(m[0], m[1])

        def PE(ins):
            return c_pe.done(ins)

        def A(ins):
            return c_act.done(ins)

        def V(ins):
            return c_dve.done(ins)

        l_xs = Count("load_xs")
        l_x = [Count(f"load_x{n}") for n in range(2)]
        l_w = [Count(f"load_w{n}") for n in range(2)]
        l_xsb = [Count(f"load_xs_b{b}") for b in range(GB)]
        l_wr = [Count(f"load_wr{n}") for n in range(3)]
        l_c = [Count(f"load_c{n}") for n in range(4)]
        l_x1 = [Count(f"load_x1_{n}") for n in range(2)]
        s_xt = Count("store_xt")
        s_x1 = [Count(f"store_x1_{n}") for n in range(2)]
        s_at = [Count(f"store_at{n}") for n in range(2)]
        s_out = [Count(f"store_out{n}") for n in range(2)]

        def split(dst_h, dst_l, src, src_ready, dst_free, later=1, low_on=dve):
            free = list(dst_free)
            wait(act, *src_ready, *free)
            ms = [A(act.activation(dst_h, src, ACT.Copy))]

            def low():
                wait(low_on, *src_ready, *free, ms[0])
                low_ = low_on.tensor_tensor(dst_l, src, dst_h.bitcast(f32), ALU.subtract)
                ms.append(V(low_) if low_on is dve else c_pool.done(low_))
            if later:
                at(place[0] + later, low)
            else:
                low()
            return ms

        m_ix = l_c[2].done(sp.dma_start(ix[:], idx), 16)
        l_x0 = [Count(f"load_x0_{b}") for b in range(GB)]
        x0_ready = [None] * GB

        def load_x0(b):
            dst = XS[:, :, b * 128:(b + 1) * 128]
            x0_ready[b] = l_x0[b].done(sp.dma_start(dst, x[b].rearrange("p (d s) -> p d s", d=DC)), 16)
        load_x0(0)
        m_ident = l_c[1].done(sp.dma_start(ident[:], ident_d), 16)
        wait(dve, m_ix)
        m = V(dve.tensor_scalar(ix2[:], ix[:], 0, NW, ALU.is_lt, ALU.mult))
        wait(dve, m)
        m = V(dve.tensor_tensor(ix[:], ix[:], ix2[:], ALU.add))
        wait(dve, m)
        m_ix = V(dve.tensor_scalar(ix2[:], ix[:], 0, NW - 1, ALU.max, ALU.min))
        m_kz = c_pool.done(pool.memset(KH[:].bitcast(f32), 0.0))
        m_kz = c_pool.done(pool.memset(KL[:].bitcast(f32), 0.0))
        m_tz = c_pool.done(pool.memset(TP[:], 0.0))

        stage = [(WR[n][:], l_wr[n], []) for n in range(3)]
        w_ready = [[None] * DC for _ in range(3)]
        w_free = [[] for _ in range(3)]
        n_wr = [0]

        def load_weight(slot, src, half, d, stages):
            tile, loads, free = stages[n_wr[0] % len(stages)]
            n_wr[0] += 1
            wait(sp, *[m for ms in free for m in ms])
            loaded = loads.done(sp.dma_start(tile, src[d * 128:(d + 1) * 128, half * 512:(half + 1) * 512]), 16)

            def finish():
                ms = split(WH[slot][:, d, :], WL[slot][:, d, :], tile, [loaded], w_free[slot],
                           low_on=pool if d in (1, 3, 5, 7) else dve)
                w_ready[slot][d] = ms
                free.clear()
                free.append(ms)
            return finish

        todo = []
        place = [0]
        order = [0]

        def at(p, stage):
            order[0] += 1
            todo.append((max(p, place[0]), order[0], stage))

        def hook():
            place[0] += 1
            while True:
                ready = [t for t in todo if t[0] <= place[0]]
                if not ready:
                    return
                t = min(ready)
                todo.remove(t)
                t[2]()

        def weights_at(p, slot, src, half, every=2, lag=4, stages=stage, chunks=range(DC)):
            for d in chunks:
                def start(d=d, p=p):
                    fin = load_weight(slot, src, half, d, stages)
                    at(p + every * d + lag, fin)
                at(p + every * d, start)

        pv_free = [[], []]
        x_free, w0_free = [[], []], [[], []]
        h_free, wh_free, lp_free = [[]], [[]], [[]]
        xs_free = [[] for _ in range(GB)]
        xs_ready = [[] for _ in range(GB)]

        def layer0(g, b, load_p, p, offsets=(4, 5, 7, 10, 13), start=False):
            bb, z = g * GB + b, b % 2
            xb, wb = xr[z], wr[z]
            tok = slice(b * 128, (b + 1) * 128)
            box = {"x1": [None, None]}
            banks = (LP, PV[1]) if start else (LP, LP)
            free_of = (lp_free, pv_free) if start else (lp_free, lp_free)
            key = (0, 1) if start else (0, 0)

            def x_half(h):
                if start:
                    return XS[:, h * 4:h * 4 + 4, tok]
                return xb[:, h * 512:(h + 1) * 512].rearrange("p (k s) -> p k s", k=4)

            def four(tile):
                return tile.rearrange("p (k s) -> p k s", k=4)

            def load():
                wait(sp, *x_free[z])
                box["x"] = l_x[z].done(sp.dma_start(xb[:], x[bb]), 16)
                load_w()

            def load_w():
                wait(sp, m_ix, *w0_free[z])
                r = sp.value_load(ix2[0:1, bb:bb + 1], min_val=0, max_val=NW - 1)
                box["w"] = l_w[z].done(sp.dma_start(wb[:], w0[bass.ds(r, 1), :, :].rearrange("o c d -> (o c) d")), 16)

            def split_w():
                if start:
                    box["x"] = x0_ready[b]
                    split_x(0)
                box["ws"] = split(wh[:], wl[:], wb[:], [box["w"]], wh_free[0])
                w0_free[z] = box["ws"]
                if not start:
                    split_x(0)

            def split_x(h):
                box["xs"] = split(four(xh[:]), four(xl[:]), x_half(h), [box["x"]], h_free[0])

            def half_a(h):
                bank = banks[h]
                wait(pe, *box["ws"], *box["xs"], *free_of[h][key[h]])
                pe.matmul(bank[:], wh[:], xh[:], start=True, stop=False)
                pe.matmul(bank[:], wh[:], xl[:], start=False, stop=False)
                mm = PE(pe.matmul(bank[:], wl[:], xh[:], start=False, stop=True))
                h_free[0] = [mm]
                wait(dve, mm, *(x_free[z] if start else ()))
                box["x1"][h] = V(dve.tensor_tensor(four(xb[:, h * 512:(h + 1) * 512]), four(bank[:]), x_half(h), ALU.add))
                free_of[h][key[h]] = [box["x1"][h]]
                if h == 1:
                    wh_free[0] = [mm]
                    wait(sp, *box["x1"])
                    box["st"] = s_x1[z].done(sp.dma_start(x1_d[bb], xb[:]), 16)

            def half_b(h):
                bank = banks[h]
                wait(pe, box["x1"][h], m_ident)
                for k in range(4):
                    t = h * 4 + k
                    mm = pe.transpose(bank[:, k * 128:(k + 1) * 128], xb[:, t * 128:(t + 1) * 128], ident[:])
                mm = PE(mm)
                wait(act, mm, *xs_free[b])
                ev = A(act.activation(XS[:, h * 4:h * 4 + 4, tok], four(bank[:]), ACT.Copy))
                free_of[h][key[h]] = [ev]
                xs_ready[b].append(ev)
                if start:
                    split_xt_half(b, h, ev)
                if h == 1:
                    x_free[z] = [mm, box["st"]]
                    wait(sp, *xs_ready[b])
                    dst = xt_d[g].rearrange("p (d t) -> p d t", d=DC)[:, :, tok]
                    st_xt[:] = [s_xt.done(sp.dma_start(dst, XS[:, :, tok]), 16)]

            at(load_p, load_w if start else load)
            at(p, split_w)
            at(p + offsets[0], lambda: half_a(0))
            at(p + offsets[1], lambda: split_x(1))
            at(p + offsets[2], lambda: half_b(0))
            at(p + offsets[3], lambda: half_a(1))
            at(p + offsets[4], lambda: half_b(1))

        st_xt = []

        x_ready = [[None] * GB for _ in range(DC)]

        def split_xt(d, free):
            ready = [m for r in xs_ready for m in r]
            ms = split(XH[:, d, :], XL[:, d, :], XS[:, d, :], ready, free, low_on=pool if d < 4 else dve)
            for b in range(GB):
                x_ready[d][b] = ms
            return ms

        def split_xt_part(b, chunks, ready, free):
            cols = slice(b * 128, (b + 1) * 128)
            ms = split(XH[:, chunks, cols], XL[:, chunks, cols], XS[:, chunks, cols], ready, free)
            for d in range(chunks.start, chunks.stop):
                x_ready[d][b] = ms
            return ms

        def split_xt_half(b, h, ready):
            split_xt_part(b, slice(4 * h, 4 * h + 4), [ready], [])

        def split_xt_batch(b, free):
            return split_xt_part(b, slice(0, DC), xs_ready[b], free)

        def reload_xs(src, g, marks, extra=()):
            wait(sp, *marks, *extra)
            m = l_xs.done(sp.dma_start(XS[:].rearrange("p d t -> p (d t)"), src[g]), 16)
            for b in range(GB):
                xs_ready[b][:] = [m]

        nblk = [0]
        pj_free = [[], [], []]

        def block(lhs, rhs, ready):
            n = nblk[0] % 3
            nblk[0] += 1
            wait(pe, *pj_free[n])
            for d in range(DC):
                wait(pe, *ready(d))
                (lh, ll), (rh, rl) = lhs(d), rhs(d)
                pe.matmul(PJ[n][:], lh, rh, start=(d == 0), stop=False)
                pe.matmul(PJ[n][:], lh, rl, start=False, stop=False)
                mm = pe.matmul(PJ[n][:], ll, rh, start=False, stop=(d == DC - 1))
                if d == DC - 1:
                    mm = PE(mm)
                hook()
            return n, mm

        v_ready, v_free = [None] * GB, [[] for _ in range(GB)]
        q_ready, k_ready = [None], [None]
        q_free, k_free = [[]], [[]]

        def row_block(slot, b):
            cols = slice(b * 128, (b + 1) * 128)
            return block(lambda d: (XH[:, d, cols], XL[:, d, cols]),
                         lambda d: (WH[slot][:, d, :], WL[slot][:, d, :]),
                         lambda d: [*w_ready[slot][d], *x_ready[d][b]])

        def col_block(slot, c):
            cols = slice(c * 128, (c + 1) * 128)
            return block(lambda d: (WH[slot][:, d, cols], WL[slot][:, d, cols]),
                         lambda d: (XH[:, d, :], XL[:, d, :]),
                         lambda d: [*w_ready[slot][d], *[m for b in range(GB) for m in x_ready[d][b]]])

        v_read = [0] * GB

        def v_block(b, later=0):
            n, mm = row_block(2, b)
            w_free[2] = [mm]

            def empty():
                v_ready[b] = split(VH[:, b, :], VL[:, b, :], PJ[n][:], [mm], v_free[b])
                pj_free[n] = v_ready[b]
            p = max(place[0] + later, v_read[b])
            if p > place[0]:
                at(p, empty)
            else:
                empty()

        def q_empty(n, mm, later=0):
            w_free[0] = [mm]

            def empty():
                q_ready[0] = pj_free[n] = split(QH[:], QL[:], PJ[n][:], [mm], q_free[0])
            if later:
                at(place[0] + later, empty)
            else:
                empty()

        def k_empty(n, mm):
            w_free[1] = [mm]
            pj = PJ[n][:].rearrange("p (b s) -> p b s", b=GB)
            free = list(k_free[0])
            wait(act, mm, m_kz, *free)
            parts = [(slice(64 * h, 64 * h + 64), slice(128 * h, 128 * h + 128)) for h in range(2)]
            ms = [A(act.activation(KH[r, :, k], pj[r], ACT.Copy)) for r, k in parts]

            def low():
                wait(dve, mm, m_kz, *free)
                for h, (r, k) in enumerate(parts):
                    wait(dve, ms[h])
                    ms.append(V(dve.tensor_tensor(KL[r, :, k], pj[r], KH[r, :, k].bitcast(f32), ALU.subtract)))
            at(place[0] + 1, low)
            k_ready[0] = ms
            pj_free[n] = ms

        def last_blocks(c):
            banks = [nblk[0] % 3, (nblk[0] + 1) % 3]
            nblk[0] += 2
            cols = slice(c * 128, (c + 1) * 128)

            def step(slot, d):
                n = banks[slot]
                if d == 0:
                    wait(pe, *pj_free[n])
                wait(pe, *w_ready[slot][d], *[m for b in range(GB) for m in x_ready[d][b]])
                lh, ll, rh, rl = WH[slot][:, d, cols], WL[slot][:, d, cols], XH[:, d, :], XL[:, d, :]
                pe.matmul(PJ[n][:], lh, rh, start=(d == 0), stop=False)
                pe.matmul(PJ[n][:], lh, rl, start=False, stop=False)
                mm = pe.matmul(PJ[n][:], ll, rh, start=False, stop=(d == DC - 1))
                if slot == 1:
                    mm = PE(mm)
                    split_xt(d, [mm])
                elif d == DC - 1:
                    mm = PE(mm)
                hook()
                return mm

            for i in range(DC + 2):
                if i < DC:
                    mm = step(0, i)
                    if i == DC - 1:
                        q_empty(banks[0], mm)
                if i >= 2:
                    mm = step(1, i - 2)
            k_empty(banks[1], mm)

        sc_free = [[], []]
        tp_free, pp_free, pth_free = [[]], [[] for _ in range(GB)], [[], []]
        at_free = [[], []]
        n_at = [0]
        at_done = [[] for _ in range(NG)]
        tri = [(i, j) for i in range(4) for j in range(i + 1)]

        def attention(g, ph, c, p0, places=(0, 1, 5, 6), lags=(2, 4, 5, 7, 8, 12)):
            an = n_at[0] % 2
            n_at[0] += 1
            ev = []

            def unit(u, box):
                z = u % 2
                bank = SC[z]

                def scores():
                    cols = slice(u * 128, (u + 1) * 128)
                    wait(pe, *q_ready[0], *k_ready[0], *sc_free[z])
                    pe.matmul(bank[:, 0:256], QH[:, cols], KH[:, u, :], start=True, stop=False)
                    pe.matmul(bank[:, 0:256], QH[:, cols], KL[:, u, :], start=False, stop=False)
                    mm = PE(pe.matmul(bank[:, 0:256], QL[:, cols], KH[:, u, :], start=False, stop=True))
                    if u == GB - 1:
                        q_free[0], k_free[0] = [mm], [mm]
                    wait(dve, mm, *m_mask, *m_beta, *pp_free[u])
                    ms = V(dve.scalar_tensor_tensor(
                        out=PP[u], in0=bank[:, 0:256].rearrange("p (h k) -> p h k", h=2), scalar=beta[:, g * GB + u:g * GB + u + 1],
                        in1=mask[:].unsqueeze(1).to_broadcast([128, 2, 128]), op0=ALU.mult, op1=ALU.add))
                    sc_free[z] = [ms]
                    wait(dve, ms)
                    box["mx"] = V(dve.tensor_reduce(st[:, u, 0:2], PP[u], AX, ALU.max, negate=True))

                def exps():
                    wait(act, box["mx"])
                    for h in range(2):
                        me = A(act.activation(PP[u][:, h, :], PP[u][:, h, :], ACT.Exp, bias=st[:, u, h:h + 1],
                                              scale=1.0, accum_out=st[:, u, 2 + h:3 + h]))
                    wait(dve, me)
                    box["r"] = V(dve.reciprocal(st[:, u, 4:6], st[:, u, 2:4]))

                def norm():
                    wait(act, box["r"])
                    for h in range(2):
                        box["n"] = A(act.activation(PP[u][:, h, :], PP[u][:, h, :], ACT.Copy,
                                                    scale=st[:, u, 4 + h:5 + h]))

                def halves():
                    box["p"] = split(PTH[z][:], PTL[z][:], TP[:, z], [box["t"], m_tz], pth_free[z], low_on=pool)
                    tp_free[0].append(box["p"])

                def values():
                    cc, k = slice(c * 128, (c + 1) * 128), u // 2
                    wait(pe, *box["p"], *v_ready[u], *pv_free[k])
                    out_ = PV[k][:, z * 256:z * 256 + 256]
                    pe.matmul(out_, VH[:, u, cc], PTH[z][:].rearrange("p h k -> p (h k)"), start=True, stop=False)
                    pe.matmul(out_, VH[:, u, cc], PTL[z][:].rearrange("p h k -> p (h k)"), start=False, stop=False)
                    mm = PE(pe.matmul(out_, VL[:, u, cc], PTH[z][:].rearrange("p h k -> p (h k)"), start=False, stop=True))
                    pth_free[z] = [mm]
                    v_free[u] = [mm]
                    if z:
                        pv = PV[k][:].rearrange("p (u h k) -> p u h k", u=2, h=2)
                        dst = AT[an][:].rearrange("p (b s) -> p b s", b=GB)[:, u - 1:u + 1, :]
                        wait(act, mm, *at_free[an])
                        e0 = A(act.activation(dst[0:64], pv[0:64, :, 0, :], ACT.Copy))
                        e1 = A(act.activation(dst[64:128], pv[64:128, :, 1, :], ACT.Copy))
                        ev.extend([e0, e1])
                        pv_free[k] = [e0, e1]
                    if u == GB - 1:
                        wait(sp, *ev)
                        j = ph * NC + c
                        m = s_at[an].done(sp.dma_start(at_d[g][:, j * T:(j + 1) * T], AT[an][:]), 16)
                        at_free[an] = [m]
                        at_done[g].append(m)

                p = p0 + places[u]
                at(p, scores)
                at(p + lags[0], exps)
                at(p + lags[1], norm)
                return halves, values

            for u in range(0, GB, 2):
                boxes = [{}, {}]
                stages = [unit(u + z, boxes[z]) for z in range(2)]

                def turn(part, u=u, boxes=boxes):
                    if part == 0:
                        wait(dve, boxes[0]["n"], boxes[1]["n"], m_tz, *[m for ms in tp_free[0] for m in ms])
                        tp_free[0] = []
                    for i, j in tri[5 * part:5 * part + 5]:
                        m = V(dve.transpose(TP[32 * j:32 * j + 32, :, :, 32 * i:32 * i + 32],
                                            PPT[32 * i:32 * i + 32, u:u + 2, :, 32 * j:32 * j + 32]))
                    if part == 1:
                        pp_free[u] = pp_free[u + 1] = [m]
                        boxes[0]["t"] = boxes[1]["t"] = m

                p = p0 + places[u + 1]
                at(p + lags[2], lambda f=turn: f(0))
                at(p + lags[3], lambda f=turn: f(1))
                for z in range(2):
                    at(p + lags[4] + z, stages[z][0])
                    at(p + lags[5] + z, stages[z][1])
                    if c == NC - 1:
                        v_read[u + z] = p + lags[5] + z + 1

        FIRST = 7
        spare = [AT[0][:], AT[1][:], xr[1][:, 0:512], xr[1][:, 512:1024],
                 PPT[:, 0:2].rearrange("p u h k -> p (u h k)")]
        early = stage + [(t, Count(f"load_spare{n}"), []) for n, t in enumerate(spare)]
        weights_at(0, 2, wv, 0, every=0, lag=5, stages=early, chunks=range(0, 4))
        for b in range(GB):
            if b:
                at(0, lambda b=b: load_x0(b))
            at_w = (0, 0, 10, 19)[b]
            if b == 1:
                at(0, lambda: weights_at(0, 2, wv, 0, every=0, lag=5, stages=early, chunks=range(4, DC)))
            layer0(0, b, at_w, (1, 8, 13, 22)[b], offsets=(2, 2, 3, 4, 5) if b == 0 else (2, 2, 4, 4, 7), start=True)
        def load_consts():
            box = [l_c[0].done(sp.dma_start(mask[:], mask_d), 16),
                   l_c[3].done(sp.dma_start(beta[:], cond.to_broadcast([128, B])), 16)]
            m_mask.append(box[0])
            at(place[0] + 4, lambda: (wait(dve, box[1]), m_beta.append(V(dve.tensor_scalar(beta[:], beta[:], 4.0, HD ** -0.5, ALU.min, ALU.mult)))))
        m_mask, m_beta = [], []
        at(2, load_consts)
        weights_at(FIRST + 5, 0, wq, 0)
        weights_at(FIRST + 25, 1, wk, 0)

        def spare_free():
            at_free[0], at_free[1] = list(early[3][2][0]), list(early[4][2][0])
            x_free[1] = [*early[5][2][0], *early[6][2][0]]
            pp_free[0] = pp_free[1] = list(early[7][2][0])
        at(FIRST, spare_free)
        while place[0] < FIRST:
            hook()

        for ph in range(2):
            for g in range(NG):
                first, last = ph == 0 and g == 0, g == NG - 1
                base = place[0]
                xs_read = [m for d in range(DC) for m in (x_ready[d][0] or ())]
                if ph == 0 and not last:
                    if not first:
                        for b in range(GB):
                            xs_free[b] = xs_read + st_xt
                            xs_ready[b][:] = []
                            layer0(g + 1, b, base + (2, 15, 33, 51)[b], base + 8 + 18 * b)
                elif ph == 0:
                    at(base + 36, lambda m=xs_read: reload_xs(xt_d, 0, m, st_xt))
                elif not last:
                    at(base + 36, lambda m=xs_read, g=g: reload_xs(xt_d, g + 1, m))
                else:
                    at(base + 36, lambda m=xs_read: reload_xs(at_d, 0, m, at_done[0]))
                if first:
                    for b in range(GB):
                        layer0(1, b, base + 33 + 10 * b, base + 39 + 10 * b, offsets=(5, 5, 8, 10, 13))
                for b in range(1 if g else GB):
                    v_block(b, 12 if g else 0)
                if first:
                    for b in range(GB):
                        xs_free[b] = [*x_ready[0][b], *x_ready[DC - 1][b], *st_xt]
                        xs_ready[b][:] = []
                for c in range(NC - 1):
                    n, mm = col_block(0, c)
                    q_empty(n, mm, Q_LATER)
                    n, mm = col_block(1, c)
                    k_empty(n, mm)
                    attention(g, ph, c, place[0] + 4, (1, 2, 15, 16) if g and c == 0 else (0, 1, 8, 9))
                    if g and c == 0:
                        for b in range(1, GB):
                            v_block(b)
                    if last and c == 0:
                        weights_at(place[0] + 2, 2, *((wv, 1) if ph == 0 else (wo, 0)))
                last_blocks(NC - 1)
                attention(g, ph, NC - 1, place[0] + 6, (0, 1, 8, 9))
                if last:
                    weights_at(place[0] + 2, 0, *((wq, 1) if ph == 0 else (wo, 1)))
                if last and ph == 0:
                    weights_at(place[0] + 18, 1, wk, 1)

        x1_free = [x_free[0], x_free[1]]
        o_free = [x_free[0], x_free[1]]
        n_out = 0
        xs_read = [m for d in range(DC) for m in x_ready[d][0]]
        stored_x1 = [(c.sem, c.n) for c in s_x1]

        def xs_batch(g, b, marks):
            wait(sp, *marks, *at_done[g])
            cols = slice(b * 128, (b + 1) * 128)
            src = at_d[g].rearrange("p (d t) -> p d t", d=DC)[:, :, cols]
            xs_ready[b][:] = [l_xsb[b].done(sp.dma_start(XS[:, :, cols], src), 16)]

        for b in range(GB):
            at(place[0] + 20 + 2 * b, lambda b=b: xs_batch(1, b, xs_read))
        for g in range(NG):
            turns = [(b, h) for b in range(GB) for h in range(2)]
            if g == 0:
                turns.sort(key=lambda t: t[1])
            for b, half in turns:
                bb, slot = g * GB + b, (2, 0)[half]
                i = n_out % 2
                n_out += 1
                cols = slice(half * 512, (half + 1) * 512)
                wait(sp, *x1_free[i], *stored_x1)
                loaded = l_x1[i].done(sp.dma_start(xr[i][:, 0:512], x1_d[bb][:, cols]), 16)
                n, mm = row_block(slot, b)
                wait(dve, mm, loaded, *o_free[i])
                ev = V(dve.tensor_tensor(xr[i][:, 512:1024], PJ[n][:], xr[i][:, 0:512], ALU.add))
                pj_free[n], x1_free[i] = [ev], [ev]
                wait(sp, ev)
                o_free[i] = [s_out[i].done(sp.dma_start(out[bb][:, cols], xr[i][:, 512:1024]), 16)]
                if half == 1 and g + 1 < NG:
                    ms = split_xt_batch(b, [mm])
                    if g + 2 < NG:
                        at(place[0] + 2, lambda g=g, b=b, ms=ms: xs_batch(g + 2, b, ms))
        for c in [*s_out, *s_at, *s_x1, s_xt]:
            wait(sp, (c.sem, c.n))


_OUT = ((B, S, D), "float32")


def kernel(x, itok_B_1_198, cond_1, L0_cond_weights, L1_cond_Wq, L1_cond_Wk, L1_cond_Wv, L1_cond_Wo):
    import concourse.bacc as bacc
    from concourse.bass_utils import run_bass_kernel_spmd

    f = np.float32
    rows = np.arange(128)
    arrays = {
        "x": np.ascontiguousarray(x),
        "idx": np.ascontiguousarray(itok_B_1_198).reshape(1, B),
        "cond": np.ascontiguousarray(cond_1).reshape(1, B),
        "w0": np.ascontiguousarray(L0_cond_weights),
        "wq": np.ascontiguousarray(np.asarray(L1_cond_Wq).T),
        "wk": np.ascontiguousarray(np.asarray(L1_cond_Wk).T),
        "wv": np.ascontiguousarray(np.asarray(L1_cond_Wv).T),
        "wo": np.ascontiguousarray(np.asarray(L1_cond_Wo).T),
        "mask": np.where(rows[None, :] <= rows[:, None], f(0), f(NEG)).astype(f),
        "ident": np.eye(128, dtype=f),
    }
    nc = bacc.Bacc("TRN2", target_bir_lowering=False, num_devices=1)
    args = [nc.dram_tensor(n, a.shape, mybir.dt.from_np(a.dtype), kind="ExternalInput").ap() for n, a in arrays.items()]
    out = nc.dram_tensor("out", _OUT[0], mybir.dt.from_np(np.dtype(_OUT[1])), kind="ExternalOutput").ap()
    cond_attention(nc, *args, out)
    r = run_bass_kernel_spmd(nc, [arrays], core_ids=[0])
    return r.results[0]["out"]
```
